# Optimizing a Trainium2 kernel written in Bass

```python
import numpy as np
import jax
import jax.numpy as jnp

def _softmax(x, axis=-1):
    return jax.nn.softmax(x, axis=axis)

def _gelu(x):
    return jax.nn.gelu(x, approximate=True)

def _silu(x):
    return jax.nn.silu(x)

def _sigmoid(x):
    return jax.nn.sigmoid(x)

def _layernorm(x, axis=-1, eps=1e-05):
    m = jnp.mean(x, axis=axis, keepdims=True)
    v = jnp.var(x, axis=axis, keepdims=True)
    return (x - m) / jnp.sqrt(v + eps)

def _scatter_add(tgt, idx, src, axis=0):
    return tgt.at[idx].add(src)

def _segment_sum(src, seg, n):
    return jax.ops.segment_sum(src, seg, n)
kernel_name = 'mk_prb_d2_jaxref_r8_74544e'

def setup_inputs(seed: int=0):
    np.random.seed(seed)
    _w = jnp.asarray

    def _L0_attn_setup():
        import jax, jax.numpy as jnp
        import numpy as np
        from jax import lax
        B, L, D_MODEL = (2, 128, 128)
        D_INNER, D_STATE, D_CONV = (256, 16, 4)
        DT_RANK = 64
        key = jax.random.key(seed)
        ks = jax.random.split(key, 10)
        s = lambda k, shp, sc=0.02: jax.random.normal(k, shp, jnp.float32) * sc
        A = jnp.tile(jnp.arange(1, D_STATE + 1, dtype=jnp.float32), (D_INNER, 1))
        return {'x': s(ks[0], (B, L, D_MODEL), 1.0), 'in_proj_w': s(ks[1], (2 * D_INNER, D_MODEL)), 'conv_w': s(ks[2], (D_INNER, 1, D_CONV), 0.1), 'conv_b': s(ks[3], (D_INNER,), 0.1), 'x_proj_w': s(ks[4], (DT_RANK + 2 * D_STATE, D_INNER)), 'dt_proj_w': s(ks[5], (D_INNER, DT_RANK), 0.1), 'dt_proj_b': s(ks[6], (D_INNER,), 0.1), 'A_log': jnp.log(A), 'D': jnp.ones((D_INNER,), jnp.float32), 'out_proj_w': s(ks[7], (D_MODEL, D_INNER))}
    _L0_attn_in = _L0_attn_setup()

    def _L0_ffn_setup():
        import jax, jax.numpy as jnp
        import numpy as np
        B, S, H, E, DFF = (4, 512, 128, 8, 512)
        key = jax.random.key(seed)
        k0, k1, k2, k3 = jax.random.split(key, 4)
        hidden_states = jax.random.normal(k0, (B, S, H), dtype=jnp.float32)
        gate_w = jax.random.normal(k1, (E, H), dtype=jnp.float32) * 0.02
        w1 = jax.random.normal(k2, (E, H, DFF), dtype=jnp.float32) * 0.02
        b1 = jnp.zeros((E, DFF), dtype=jnp.float32)
        w2 = jax.random.normal(k3, (E, DFF, H), dtype=jnp.float32) * 0.02
        b2 = jnp.zeros((E, H), dtype=jnp.float32)
        return {'hidden_states': hidden_states, 'gate_w': gate_w, 'w1': w1, 'b1': b1, 'w2': w2, 'b2': b2}
    _L0_ffn_in = _L0_ffn_setup()

    def _L1_attn_setup():
        import jax, jax.numpy as jnp
        import numpy as np
        ALPHA = 1.2
        A = 1.0
        BANDWIDTH = 1.0
        D_INTRINSIC = 2
        SPHERE_RADIUS = 1.0
        NUM_HEADS = 16
        HIDDEN = 128
        HEAD_DIM = HIDDEN // NUM_HEADS
        EPS = 1e-07

        def _l2norm(t):
            n = jnp.sqrt(jnp.sum(t * t, axis=-1, keepdims=True))
            return t / jnp.maximum(n, 1e-12)
        key = jax.random.key(seed)
        k1, k2, k3, k4, k5 = jax.random.split(key, 5)
        B, S = (2, 256)
        scale = 0.02
        return {'x': jax.random.normal(k1, (B, S, HIDDEN), dtype=jnp.float32), 'w_qkv': jax.random.normal(k2, (3 * HIDDEN, HIDDEN), dtype=jnp.float32) * scale, 'b_qkv': jnp.zeros((3 * HIDDEN,), dtype=jnp.float32), 'w_out': jax.random.normal(k3, (HIDDEN, HIDDEN), dtype=jnp.float32) * scale, 'b_out': jnp.zeros((HIDDEN,), dtype=jnp.float32)}
    _L1_attn_in = _L1_attn_setup()

    def _L1_ffn_setup():
        import jax, jax.numpy as jnp
        import numpy as np
        DIM = 128
        DEPTH = 2
        HEADS = 8
        DIM_HEAD = 64
        WINDOW = 64
        INNER = HEADS * DIM_HEAD
        HID = int(DIM * 4 * 2 / 3)
        B, N = (2, 1024)
        QK_SCALE = 8.0

        def shift_token(t):
            t1, t2 = jnp.split(t, 2, axis=-1)
            t2 = jnp.pad(t2, ((0, 0), (1, 0), (0, 0)))[:, :-1]
            return jnp.concatenate([t1, t2], axis=-1)

        def l2norm(t):
            return t / jnp.clip(jnp.linalg.norm(t, axis=-1, keepdims=True), 1e-12)

        def rotate_half(x):
            x1, x2 = jnp.split(x, 2, axis=-1)
            return jnp.concatenate([-x2, x1], axis=-1)

        def rotary_xpos(q, k):
            n = q.shape[-2]
            half_idx = jnp.arange(0, DIM_HEAD, 2, dtype=jnp.float32)
            inv_freq = 1.0 / 10000.0 ** (half_idx / DIM_HEAD)
            t = jnp.arange(n, dtype=jnp.float32)
            freqs = t[:, None] * inv_freq[None, :]
            freqs = jnp.concatenate([freqs, freqs], axis=-1)
            base = (half_idx + 0.4 * DIM_HEAD) / (1.4 * DIM_HEAD)
            power = (t - n // 2) / float(WINDOW // 2)
            scale = base[None, :] ** power[:, None]
            scale = jnp.concatenate([scale, scale], axis=-1)
            cos, sin = (jnp.cos(freqs), jnp.sin(freqs))
            q = q * cos * scale + rotate_half(q) * sin * scale
            k = k * cos / scale + rotate_half(k) * sin / scale
            return (q, k)

        def local_attention(q, k, v):
            b, h, n, d = q.shape
            w = n // WINDOW
            bq = q.reshape(b, h, w, WINDOW, d) * QK_SCALE
            bk = k.reshape(b, h, w, WINDOW, d)
            bv = v.reshape(b, h, w, WINDOW, d)

            def look_around(t):
                p = jnp.pad(t, ((0, 0), (0, 0), (1, 0), (0, 0), (0, 0)))
                return jnp.concatenate([p[:, :, :w], p[:, :, 1:]], axis=3)
            bk, bv = (look_around(bk), look_around(bv))
            bt = jnp.arange(n).reshape(w, WINDOW)
            btp = jnp.pad(bt, ((1, 0), (0, 0)), constant_values=-1)
            btk = jnp.concatenate([btp[:w], btp[1:]], axis=1)
            sim = jnp.einsum('bhwid,bhwjd->bhwij', bq, bk)
            i = bt[:, :, None]
            j = btk[:, None, :]
            mask = (i < j) | (i > j + WINDOW) | (j == -1)
            sim = jnp.where(mask, -jnp.finfo(sim.dtype).max, sim)
            attn = jax.nn.softmax(sim, axis=-1)
            out = jnp.einsum('bhwij,bhwjd->bhwid', attn, bv)
            return out.reshape(b, h, n, d)

        def _layer(x, wqkv, qs, ksc, wo, lg, lb, w1, b1, w2, b2):
            b, n, _ = x.shape
            h = shift_token(x)
            qkv = h @ wqkv
            q, k, v = jnp.split(qkv, 3, axis=-1)
            to_heads = lambda t: t.reshape(b, n, HEADS, DIM_HEAD).transpose(0, 2, 1, 3)
            q, k, v = (to_heads(q), to_heads(k), to_heads(v))
            q = l2norm(q) * qs
            k = l2norm(k) * ksc
            q, k = rotary_xpos(q, k)
            o = local_attention(q, k, v)
            o = o.transpose(0, 2, 1, 3).reshape(b, n, INNER)
            x = x + o @ wo
            h = shift_token(x)
            mu = h.mean(-1, keepdims=True)
            var = h.var(-1, keepdims=True)
            h = (h - mu) / jnp.sqrt(var + 1e-05) * lg + lb
            h = h @ w1 + b1
            a, g = jnp.split(h, 2, axis=-1)
            h = a * jax.nn.gelu(g, approximate=False)
            x = x + h @ w2 + b2
            return x
        key = jax.random.key(seed)
        ks = jax.random.split(key, 6)
        return {'x': jax.random.normal(ks[0], (B, N, DIM), jnp.float32), 'wqkv': jax.random.normal(ks[1], (DEPTH, DIM, 3 * INNER), jnp.float32) * 0.02, 'q_scale': jnp.ones((DEPTH, DIM_HEAD), jnp.float32), 'k_scale': jnp.ones((DEPTH, DIM_HEAD), jnp.float32), 'wo': jax.random.normal(ks[2], (DEPTH, INNER, DIM), jnp.float32) * 0.02, 'ln_g': jnp.ones((DEPTH, DIM), jnp.float32), 'ln_b': jnp.zeros((DEPTH, DIM), jnp.float32), 'w1': jax.random.normal(ks[3], (DEPTH, DIM, 2 * HID), jnp.float32) * 0.02, 'b1': jnp.zeros((DEPTH, 2 * HID), jnp.float32), 'w2': jax.random.normal(ks[4], (DEPTH, HID, DIM), jnp.float32) * 0.02, 'b2': jnp.zeros((DEPTH, DIM), jnp.float32)}
    _L1_ffn_in = _L1_ffn_setup()
    _d = {'L0_attn_x': _L0_attn_in['x'], 'L0_attn_in_proj_w': _L0_attn_in['in_proj_w'], 'L0_attn_conv_w': _L0_attn_in['conv_w'], 'L0_attn_conv_b': _L0_attn_in['conv_b'], 'L0_attn_x_proj_w': _L0_attn_in['x_proj_w'], 'L0_attn_dt_proj_w': _L0_attn_in['dt_proj_w'], 'L0_attn_dt_proj_b': _L0_attn_in['dt_proj_b'], 'L0_attn_A_log': _L0_attn_in['A_log'], 'L0_attn_D': _L0_attn_in['D'], 'L0_attn_out_proj_w': _L0_attn_in['out_proj_w'], 'L0_ffn_gate_w': _L0_ffn_in['gate_w'], 'L0_ffn_w1': _L0_ffn_in['w1'], 'L0_ffn_b1': _L0_ffn_in['b1'], 'L0_ffn_w2': _L0_ffn_in['w2'], 'L0_ffn_b2': _L0_ffn_in['b2'], 'L1_attn_w_qkv': _L1_attn_in['w_qkv'], 'L1_attn_b_qkv': _L1_attn_in['b_qkv'], 'L1_attn_w_out': _L1_attn_in['w_out'], 'L1_attn_b_out': _L1_attn_in['b_out'], 'L1_ffn_wqkv': _L1_ffn_in['wqkv'], 'L1_ffn_q_scale': _L1_ffn_in['q_scale'], 'L1_ffn_k_scale': _L1_ffn_in['k_scale'], 'L1_ffn_wo': _L1_ffn_in['wo'], 'L1_ffn_ln_g': _L1_ffn_in['ln_g'], 'L1_ffn_ln_b': _L1_ffn_in['ln_b'], 'L1_ffn_w1': _L1_ffn_in['w1'], 'L1_ffn_b1': _L1_ffn_in['b1'], 'L1_ffn_w2': _L1_ffn_in['w2'], 'L1_ffn_b2': _L1_ffn_in['b2']}
    _x0 = _d['L0_attn_x']
    _d['L0_attn_x'] = jax.random.normal(jax.random.fold_in(jax.random.key(seed), 1), (16, 256, 128), dtype=_x0.dtype)
    del _x0
    return _d

def reference(L0_attn_x, L0_attn_in_proj_w, L0_attn_conv_w, L0_attn_conv_b, L0_attn_x_proj_w, L0_attn_dt_proj_w, L0_attn_dt_proj_b, L0_attn_A_log, L0_attn_D, L0_attn_out_proj_w, L0_ffn_gate_w, L0_ffn_w1, L0_ffn_b1, L0_ffn_w2, L0_ffn_b2, L1_attn_w_qkv, L1_attn_b_qkv, L1_attn_w_out, L1_attn_b_out, L1_ffn_wqkv, L1_ffn_q_scale, L1_ffn_k_scale, L1_ffn_wo, L1_ffn_ln_g, L1_ffn_ln_b, L1_ffn_w1, L1_ffn_b1, L1_ffn_w2, L1_ffn_b2):

    def _L0_attn_ref(x, in_proj_w, conv_w, conv_b, x_proj_w, dt_proj_w, dt_proj_b, A_log, D, out_proj_w):
        import jax, jax.numpy as jnp
        import numpy as np
        from jax import lax
        B, L, D_MODEL = (2, 128, 128)
        D_INNER, D_STATE, D_CONV = (256, 16, 4)
        DT_RANK = 64
        b, l, _ = x.shape
        d_inner, d_state = A_log.shape
        dt_rank = dt_proj_w.shape[1]
        d_conv = conv_w.shape[-1]
        xz = jnp.einsum('bld,ed->ble', x, in_proj_w)
        xc, z = jnp.split(xz, 2, axis=-1)
        xt = xc.transpose(0, 2, 1)
        xt = lax.conv_general_dilated(xt, conv_w, window_strides=(1,), padding=[(d_conv - 1, 0)], feature_group_count=d_inner, dimension_numbers=('NCH', 'OIH', 'NCH'))
        xt = xt + conv_b[None, :, None]
        xs = jax.nn.silu(xt.transpose(0, 2, 1))
        x_dbl = jnp.einsum('bld,rd->blr', xs, x_proj_w)
        dt, Bm, Cm = jnp.split(x_dbl, [dt_rank, dt_rank + d_state], axis=-1)
        dt = jax.nn.softplus(jnp.einsum('blr,dr->bld', dt, dt_proj_w) + dt_proj_b)
        A = -jnp.exp(A_log)
        deltaA = jnp.exp(dt[..., None] * A)
        deltaBx = dt[..., None] * Bm[:, :, None, :] * xs[..., None]

        def step(h, inputs):
            dA, dBx, c = inputs
            h = dA * h + dBx
            y = jnp.einsum('bdn,bn->bd', h, c)
            return (h, y)
        h0 = jnp.zeros((b, d_inner, d_state), xs.dtype)
        _, ys = lax.scan(step, h0, (deltaA.transpose(1, 0, 2, 3), deltaBx.transpose(1, 0, 2, 3), Cm.transpose(1, 0, 2)))
        y = ys.transpose(1, 0, 2) + D * xs
        y = y * jax.nn.silu(z)
        return jnp.einsum('bld,ed->ble', y, out_proj_w)

    def _L0_ffn_ref(hidden_states, gate_w, w1, b1, w2, b2):
        import jax, jax.numpy as jnp
        import numpy as np
        B, S, H, E, DFF = (4, 512, 128, 8, 512)
        b, s, h = hidden_states.shape
        x = hidden_states.reshape(-1, h)
        gate_logits = x @ gate_w.T
        gate_probs = jax.nn.softmax(gate_logits, axis=-1)
        expert_idx = jnp.argmax(gate_probs, axis=-1)
        expert_w = jnp.take_along_axis(gate_probs, expert_idx[:, None], axis=1)[:, 0]
        out = jnp.zeros_like(x)
        n_experts = w1.shape[0]
        for e in range(n_experts):
            ye = jax.nn.relu(x @ w1[e] + b1[e]) @ w2[e] + b2[e]
            sel = (expert_idx == e)[:, None]
            out = out + jnp.where(sel, ye * expert_w[:, None], 0.0)
        return out.reshape(b, s, h)

    def _L1_attn_ref(x, w_qkv, b_qkv, w_out, b_out):
        import jax, jax.numpy as jnp
        import numpy as np
        ALPHA = 1.2
        A = 1.0
        BANDWIDTH = 1.0
        D_INTRINSIC = 2
        SPHERE_RADIUS = 1.0
        NUM_HEADS = 16
        HIDDEN = 128
        HEAD_DIM = HIDDEN // NUM_HEADS
        EPS = 1e-07

        def _l2norm(t):
            n = jnp.sqrt(jnp.sum(t * t, axis=-1, keepdims=True))
            return t / jnp.maximum(n, 1e-12)
        B, S, H = x.shape
        qkv = x @ w_qkv.T + b_qkv
        q, k, v = jnp.split(qkv, 3, axis=-1)
        to_heads = lambda t: t.reshape(B, S, NUM_HEADS, HEAD_DIM).transpose(0, 2, 1, 3)
        q = _l2norm(to_heads(q))
        k = _l2norm(to_heads(k))
        v = to_heads(v)
        cos = jnp.einsum('bhsd,bhtd->bhst', q, k)
        g_dist = jnp.arccos(jnp.clip(cos, -1.0 + EPS, 1.0 - EPS)) * SPHERE_RADIUS
        attn_score = (1.0 + g_dist / BANDWIDTH ** 0.5) ** (-D_INTRINSIC - ALPHA)
        n_r = jnp.sum(attn_score, axis=-1)
        n_c = jnp.sum(attn_score, axis=-2)
        k_tilde = (n_r ** (-A))[..., :, None] * attn_score * (n_c ** (-A))[..., None, :]
        probs = k_tilde / jnp.maximum(jnp.sum(k_tilde, axis=-1, keepdims=True), 1e-12)
        out = jnp.einsum('bhst,bhtd->bhsd', probs, v)
        out = out.transpose(0, 2, 1, 3).reshape(B, S, H)
        return out @ w_out.T + b_out

    def _L1_ffn_ref(x, wqkv, q_scale, k_scale, wo, ln_g, ln_b, w1, b1, w2, b2):
        import jax, jax.numpy as jnp
        import numpy as np
        DIM = 128
        DEPTH = 2
        HEADS = 8
        DIM_HEAD = 64
        WINDOW = 64
        INNER = HEADS * DIM_HEAD
        HID = int(DIM * 4 * 2 / 3)
        B, N = (2, 1024)
        QK_SCALE = 8.0

        def shift_token(t):
            t1, t2 = jnp.split(t, 2, axis=-1)
            t2 = jnp.pad(t2, ((0, 0), (1, 0), (0, 0)))[:, :-1]
            return jnp.concatenate([t1, t2], axis=-1)

        def l2norm(t):
            return t / jnp.clip(jnp.linalg.norm(t, axis=-1, keepdims=True), 1e-12)

        def rotate_half(x):
            x1, x2 = jnp.split(x, 2, axis=-1)
            return jnp.concatenate([-x2, x1], axis=-1)

        def rotary_xpos(q, k):
            n = q.shape[-2]
            half_idx = jnp.arange(0, DIM_HEAD, 2, dtype=jnp.float32)
            inv_freq = 1.0 / 10000.0 ** (half_idx / DIM_HEAD)
            t = jnp.arange(n, dtype=jnp.float32)
            freqs = t[:, None] * inv_freq[None, :]
            freqs = jnp.concatenate([freqs, freqs], axis=-1)
            base = (half_idx + 0.4 * DIM_HEAD) / (1.4 * DIM_HEAD)
            power = (t - n // 2) / float(WINDOW // 2)
            scale = base[None, :] ** power[:, None]
            scale = jnp.concatenate([scale, scale], axis=-1)
            cos, sin = (jnp.cos(freqs), jnp.sin(freqs))
            q = q * cos * scale + rotate_half(q) * sin * scale
            k = k * cos / scale + rotate_half(k) * sin / scale
            return (q, k)

        def local_attention(q, k, v):
            b, h, n, d = q.shape
            w = n // WINDOW
            bq = q.reshape(b, h, w, WINDOW, d) * QK_SCALE
            bk = k.reshape(b, h, w, WINDOW, d)
            bv = v.reshape(b, h, w, WINDOW, d)

            def look_around(t):
                p = jnp.pad(t, ((0, 0), (0, 0), (1, 0), (0, 0), (0, 0)))
                return jnp.concatenate([p[:, :, :w], p[:, :, 1:]], axis=3)
            bk, bv = (look_around(bk), look_around(bv))
            bt = jnp.arange(n).reshape(w, WINDOW)
            btp = jnp.pad(bt, ((1, 0), (0, 0)), constant_values=-1)
            btk = jnp.concatenate([btp[:w], btp[1:]], axis=1)
            sim = jnp.einsum('bhwid,bhwjd->bhwij', bq, bk)
            i = bt[:, :, None]
            j = btk[:, None, :]
            mask = (i < j) | (i > j + WINDOW) | (j == -1)
            sim = jnp.where(mask, -jnp.finfo(sim.dtype).max, sim)
            attn = jax.nn.softmax(sim, axis=-1)
            out = jnp.einsum('bhwij,bhwjd->bhwid', attn, bv)
            return out.reshape(b, h, n, d)

        def _layer(x, wqkv, qs, ksc, wo, lg, lb, w1, b1, w2, b2):
            b, n, _ = x.shape
            h = shift_token(x)
            qkv = h @ wqkv
            q, k, v = jnp.split(qkv, 3, axis=-1)
            to_heads = lambda t: t.reshape(b, n, HEADS, DIM_HEAD).transpose(0, 2, 1, 3)
            q, k, v = (to_heads(q), to_heads(k), to_heads(v))
            q = l2norm(q) * qs
            k = l2norm(k) * ksc
            q, k = rotary_xpos(q, k)
            o = local_attention(q, k, v)
            o = o.transpose(0, 2, 1, 3).reshape(b, n, INNER)
            x = x + o @ wo
            h = shift_token(x)
            mu = h.mean(-1, keepdims=True)
            var = h.var(-1, keepdims=True)
            h = (h - mu) / jnp.sqrt(var + 1e-05) * lg + lb
            h = h @ w1 + b1
            a, g = jnp.split(h, 2, axis=-1)
            h = a * jax.nn.gelu(g, approximate=False)
            x = x + h @ w2 + b2
            return x
        for l in range(DEPTH):
            x = _layer(x, wqkv[l], q_scale[l], k_scale[l], wo[l], ln_g[l], ln_b[l], w1[l], b1[l], w2[l], b2[l])
        return x
    x = L0_attn_x
    xn = _layernorm(x, axis=-1)
    x = x + _L0_attn_ref(xn, L0_attn_in_proj_w, L0_attn_conv_w, L0_attn_conv_b, L0_attn_x_proj_w, L0_attn_dt_proj_w, L0_attn_dt_proj_b, L0_attn_A_log, L0_attn_D, L0_attn_out_proj_w) + _L0_ffn_ref(xn, L0_ffn_gate_w, L0_ffn_w1, L0_ffn_b1, L0_ffn_w2, L0_ffn_b2)
    xn = _layernorm(x, axis=-1)
    x = x + _L1_attn_ref(xn, L1_attn_w_qkv, L1_attn_b_qkv, L1_attn_w_out, L1_attn_b_out) + _L1_ffn_ref(xn, L1_ffn_wqkv, L1_ffn_q_scale, L1_ffn_k_scale, L1_ffn_wo, L1_ffn_ln_g, L1_ffn_ln_b, L1_ffn_w1, L1_ffn_b1, L1_ffn_w2, L1_ffn_b2)
    return x

_drawn_inputs = setup_inputs


def setup_inputs(seed=0):
    import zlib

    import numpy as np

    out = dict(_drawn_inputs(seed))
    spreads = {'L0_attn_D': (1.0, 0.2),
     'L0_ffn_b1': (0.0, 0.1),
     'L0_ffn_b2': (0.0, 0.1),
     'L1_attn_b_qkv': (0.0, 0.1),
     'L1_attn_b_out': (0.0, 0.1),
     'L1_ffn_q_scale': (1.0, 0.2),
     'L1_ffn_k_scale': (1.0, 0.2),
     'L1_ffn_ln_g': (1.0, 0.2),
     'L1_ffn_ln_b': (0.0, 0.1),
     'L1_ffn_b1': (0.0, 0.1),
     'L1_ffn_b2': (0.0, 0.1)}
    factors = {}
    for name, (base, spread) in spreads.items():
        noise = np.random.default_rng([zlib.crc32(name.encode()), seed]).standard_normal(out[name].shape)
        drawn = base * np.exp(spread * noise) if base else spread * noise
        out[name] = jnp.asarray(drawn.astype(out[name].dtype))
    for name, factor in factors.items():
        out[name] = (out[name] * factor).astype(out[name].dtype)
    return out
```

```python
import numpy as np
import concourse.bass as bass
from concourse import mybir
from contextlib import ExitStack

F32, BF16 = mybir.dt.float32, mybir.dt.bfloat16
ALU = mybir.AluOpType
ACT = mybir.ActivationFunctionType
AX = mybir.AxisListType

P = 128
SEQS, L, DM = 16, 256, 128
NPAIR = SEQS // 2
T = 2 * L
TT = T // P
DI, NS, DC, DR = 256, 16, 4, 64
CH = DI // P
NG = 4
NE, DFF = 8, 512
FJ = DFF // P
GH, GD = 16, 8
HB = 4
LAY, LH, LD, WIN = 2, 8, 64, 64
INNER = LH * LD
HID = 341
HC = [128, 128, 85]
SW = P + L
LN_EPS = 1e-5
NEG = -3.0e38
ARENA = 31600


class Marks:

    TABLES = {ACT.Exp: "natural_log_exp_and_others", ACT.Ln: "natural_log_exp_and_others",
              ACT.Tanh: "sigmoid_and_others", ACT.Arctan: "sigmoid_and_others", ACT.Gelu: "gelu_and_others",
              ACT.Silu: "silu_and_others", ACT.Sqrt: "sqrt_and_others"}

    def __init__(self, nc, ctx):
        self.nc = nc
        names = ["pe", "act", "dve", "pool", "x", "out", "w"]
        self.sem = {n: ctx.enter_context(nc.semaphore("s_" + n)) for n in names}
        self.engine = {"pe": nc.tensor, "act": nc.scalar, "dve": nc.vector, "pool": nc.gpsimd, "sp": nc.sync}
        numbers = [s.num for s in self.sem.values()]
        self.all = range(min(numbers), max(numbers) + 1)
        self.reset()

    def reset(self):
        self.count = {n: 0 for n in self.sem}
        self.seen = {e: {} for e in self.engine}
        self.free_at = {e: 0.0 for e in self.engine}
        self.at = {}
        self.last = 0.0
        self.table = None

    def time(self, marks):
        return max([self.at.get(k, 0.0) for k in marks if k is not None], default=0.0)

    def wait(self, who, after):
        need = {}
        for mark in after:
            if mark is not None:
                need[mark[0]] = max(need.get(mark[0], 0), mark[1])
        for name, value in need.items():
            if self.seen[who].get(name, 0) < value:
                self.engine[who].wait_ge(self.sem[name], value)
                self.seen[who][name] = value

    def emit(self, who, op, after, args, kw, ns, signal=True):
        self.wait(who, after)
        ins = op(*args, **kw)
        begin = max(self.free_at[who], self.time(after) + 60)
        self.free_at[who] = self.last = begin + ns
        if signal:
            self.count[who] += 1
            ins.then_inc(self.sem[who], 1)
            self.at[(who, self.count[who])] = self.last
        return (who, self.count[who])

    def dma(self, who, name, out, in_, after=()):
        self.wait(who, after)
        self.engine[who].dma_start(out, in_).then_inc(self.sem[name], 16)
        self.count[name] += 16
        self.last = self.at[(name, self.count[name])] = self.time(after) + 2500
        return (name, self.count[name])


HELD = "held"


class Slot:

    def __init__(self, ap):
        self.ap, self.free, self.before = ap, [], []


class Ring:
    def __init__(self, aps, m):
        self.slots, self.m = [Slot(a) for a in aps], m

    def take(self):
        while True:
            idle = [s for s in self.slots if s.free is not None]
            if idle:
                s = min(idle, key=lambda q: self.m.time(q.free))
                s.before, s.free = s.free, None
                return s
            yield HELD


def run(m, *queues):
    live, todo = [], [[depth, list(gens), 0] for depth, gens in queues]
    serial = 0
    while True:
        for q in todo:
            while q[1] and q[2] < q[0]:
                live.append([max([c[0] for c in live], default=0.0) * 0.0, serial, q[1].pop(0), q, None])
                serial += 1
                q[2] += 1
        if not live:
            return
        key = lambda c: (c[0] + (2500.0 if c[4] and c[4] != m.table else 0.0), c[1])
        for c in sorted(live, key=key):
            try:
                said = next(c[2])
            except StopIteration:
                live.remove(c)
                c[3][2] -= 1
                break
            if said != HELD:
                c[0], c[4] = m.last, said
                break
        else:
            raise RuntimeError("every chain is held")


def build(nc, d, out):
    ctx = ExitStack()
    with ctx:
        m = Marks(nc, ctx)

        def sb(name, shape, dt=F32):
            return ctx.enter_context(nc.sbuf_tensor(name, shape, dt))

        banks = [ctx.enter_context(nc.psum_tensor(f"bank{i}", [P, 512], F32))[:] for i in range(8)]

        def size(ap):
            return int(np.prod(ap.shape[1:]))

        def PE(out_, lhsT, rhs, start, stop, after=(), signal=False):
            passes = 1 if rhs.dtype == BF16 else 4
            ns = passes * max(64, size(rhs)) / 2.4
            return m.emit("pe", nc.tensor.matmul, after, (out_, lhsT, rhs), dict(start=start, stop=stop), ns, signal)

        def TR(out_, in_, after=(), signal=False):
            k = in_.shape[0]
            return m.emit("pe", nc.tensor.transpose, after, (out_, in_, ident[0:k, 0:k]), {}, 4 * k / 2.4, signal)

        def A(out_, in_, func, after=(), **kw):
            need = m.TABLES.get(func)
            if need and need != m.table:
                nc.scalar.preload_act_table_set(need)
                m.table = need
                m.free_at["act"] += 1280
            return m.emit("act", nc.scalar.activation, after, (out_, in_, func), kw, 190 + size(out_) * 0.84)

        def V(op, *args, after=(), **kw):
            return m.emit("dve", op, after, args, kw, 70 + size(args[0] if isinstance(args[1], float) else args[1]) * 1.05)

        def G(op, *args, after=(), **kw):
            return m.emit("pool", op, [*after, ("pool", m.count["pool"])], args, kw, 100 + size(args[0]) * 2.2)

        v, g = nc.vector, nc.gpsimd

        def bc(ap, shape):
            return ap.broadcast_to(shape)

        def tiles(bank):
            return bank.rearrange("p (t d) -> p t d", t=TT)

        def flat2(ap):
            return ap.rearrange("p a b -> p (a b)")

        LN_EXP, TANH_ATAN = m.TABLES[ACT.Exp], m.TABLES[ACT.Tanh]
        SQRT, SILU, GELU = m.TABLES[ACT.Sqrt], m.TABLES[ACT.Silu], m.TABLES[ACT.Gelu]

        loads = []

        def load(name, shape):
            t = sb("w_" + name, shape)
            loads.append((t[:], d[name]))
            return t

        ident = load("ident", [P, P])
        w_in = load("in_projT", [P, 2 * DI])
        conv_w = load("conv_w", [P, CH, DC])
        conv_b = load("conv_b", [P, CH])
        w_dtr = load("x_projT_dt", [P, CH, DR])
        w_bc3 = load("x_projT_bc3", [P, CH, 96])
        w_dt = load("dt_projT", [DR, DI])
        dt_b = load("dt_b", [P, CH])
        a_neg = load("A_log", [P, CH, NS])
        d_skip = load("D", [P, CH])
        w_mo = load("out_projT", [P, CH, DM])
        gate = load("gateT", [P, NE])
        w1 = load("w1", [P, NE, DFF])
        b1 = load("b1", [P, NE, FJ])
        w2 = load("w2", [P, NE, FJ, DM])
        b2 = load("b2", [NE, DM])
        rank = load("rank", [P, NE])
        sel_f = load("sel", [96, 2 * NS])
        w_gqkv = load("g_qkvT", [P, 3 * DM])
        b_gqkv = load("g_b_qkv", [P, 3 * DM])
        w_go = load("g_outT", [P, DM])
        b_go = load("g_b_out", [P, DM])
        w_lqkv = load("l_wqkv", [P, LAY, 3 * INNER])
        w_lo = load("l_wo", [P, LAY, INNER // P, DM])
        ln_g = load("l_ln_g", [P, LAY])
        ln_b = load("l_ln_b", [P, LAY])
        f_w1 = load("l_w1", [P, LAY, 2 * HID])
        f_b1 = load("l_b1", [P, LAY, 2, 3])
        f_w2 = load("l_w2", [P, LAY, 3, DM])
        f_b2 = load("l_b2", [P, LAY, DM])
        rot = load("rot", [P, LAY, 2, 2, 2, LD])
        qks = load("qk_scale", [P, LAY, 2, 2, LD])
        mask = load("mask", [P, SW])
        sel = sb("sel", [96, 2 * NS], BF16)
        half = sb("half", [P, 1])
        one_b = sb("one_b", [P, 2])

        x = sb("x", [P, TT, DM])
        x1 = sb("x1", [P, TT, DM])
        xn = sb("xn", [P, TT, DM])
        xnT = sb("xnT", [P, T])
        stat6 = sb("stat6", [P, TT, 6])
        stat = sb("stat", [P, TT, 2])
        rstd = sb("rstd", [P, TT])

        arena = sb("arena", [P, ARENA])

        class Arena:
            def __init__(self):
                self.at = 0

            def get(self, *dims, dt=F32, parts=P):
                n = int(np.prod(dims))
                words = n if dt == F32 else (n + 1) // 2
                if self.at + words > ARENA:
                    raise ValueError(f"arena {self.at + words}")
                ap = arena[0:parts, self.at:self.at + words]
                self.at += words
                if dt != F32:
                    ap = ap.bitcast(dt)
                names = "abcd"[:len(dims)]
                if len(dims) > 1:
                    ap = ap.rearrange(f"p ({' '.join(names)}) -> p {' '.join(names)}",
                                      **{k: s for k, s in zip(names, dims)})
                return ap

        def ring_of(aps):
            r = Ring(aps, m)
            rings.append(r)
            return r

        rings = []

        def fence():
            nc.all_engine_barrier(sems_to_clear=m.all)
            m.reset()
            for r in rings:
                for s in r.slots:
                    s.free = []

        for n, (dst, src) in enumerate(loads):
            w_ready = m.dma("sp" if n % 2 else "act", "w", dst, src)
        V(v.memset, half[:], -0.5)
        V(v.memset, one_b[:, 0:1], 1.0)
        V(v.memset, one_b[:, 1:2], float(1.0 + np.pi / 2))
        t = A(a_neg[:], a_neg[:], ACT.Exp, after=[w_ready])
        V(v.tensor_scalar, a_neg[:], a_neg[:], -1.0, None, ALU.mult, after=[t, w_ready])
        V(v.tensor_copy, sel[:], sel_f[:])
        for l in range(LAY):
            for k in range(2):
                V(v.tensor_tensor, rot[:, l, k], rot[:, l, k],
                  bc(qks[:, l, k].unsqueeze(1), [P, 2, 2, LD]), ALU.mult)
        fence()

        def transpose4(bank, src, after):
            for tt in range(TT):
                t = TR(bank[:, tt * P:(tt + 1) * P], src[:, tt], after=after if tt == 0 else [], signal=tt == TT - 1)
            return t

        def layernorm(src, dst, ready):
            for tt in range(TT):
                t = V(v.bn_stats, stat6[:, tt], src[:, tt], after=ready)
            for tt in range(TT):
                t = V(v.bn_aggr, stat[:, tt], stat6[:, tt], after=[t])
            t = G(g.tensor_scalar, rstd[:], stat[:, :, 1], LN_EPS, None, ALU.add, after=[t])
            t = G(g.tensor_tensor, rstd[:], rstd[:], bc(half[:], [P, TT]), ALU.pow, after=[t])
            yield
            for tt in range(TT):
                r = V(v.tensor_scalar, dst[:, tt], src[:, tt], stat[:, tt, 0:1], rstd[:, tt:tt + 1],
                      ALU.subtract, ALU.mult, after=[t])
            return r

        def until(key):
            while key not in done:
                yield HELD
            return done[key]

        done = {}

        a0 = Arena()
        xcp = a0.get(CH, 2, L + DC - 1)
        xs = a0.get(CH, T)
        tmp = a0.get(CH, T)
        zs = a0.get(CH, T)
        bcr = a0.get(T, parts=96)
        bch = a0.get(T, dt=BF16, parts=96)
        bcm = a0.get(T, dt=BF16, parts=96)
        dtr = a0.get(T, parts=DR)
        dtv = a0.get(CH, T)
        du = a0.get(CH, T)
        dA = ring_of([a0.get(NG, T) for _ in range(2)])
        hB = ring_of([a0.get(NG, T) for _ in range(2)])
        Bb = ring_of([a0.get(NG, T) for _ in range(2)])
        Cb = ring_of([a0.get(NG, T)])
        hT = ring_of([a0.get(FJ, T) for _ in range(2)])
        moe = a0.get(TT, DM)
        prod = ring_of([a0.get(TT, DM)])
        lg = a0.get(TT, NE)
        ex = a0.get(TT, NE)
        me = a0.get(TT, NE)
        keyt = a0.get(TT, NE)
        r4 = a0.get(4, TT)
        meT = a0.get(T, parts=NE)
        m_ring = ring_of(banks[0:2])
        y_bank = banks[2:4]
        h_ring = ring_of(banks[4:6])
        ye_ring = ring_of(banks[6:8])

        def first(xr):
            r = yield from layernorm(x[:], xn[:], [xr])
            s = yield from m_ring.take()
            t = transpose4(s.ap, xn[:], [r] + s.before)
            s.free = [V(v.tensor_copy, xnT[:], s.ap, after=[t])]
            done["xnT"] = s.free[0]
            yield

        def mamba_in(c):
            ready = yield from until("xnT")
            o = xs[:, c].rearrange("p (s l) -> p s l", s=2)
            zero = G(g.memset, xcp[:, c, :, 0:DC - 1], 0.0)
            s = yield from m_ring.take()
            t = PE(s.ap, w_in[:, c * P:(c + 1) * P], xnT[:], True, True, after=[ready] + s.before, signal=True)
            e = A(xcp[:, c, :, DC - 1:], s.ap.rearrange("p (s l) -> p s l", s=2), ACT.Copy, after=[t, zero])
            s.free = [e]
            yield
            e = V(v.tensor_scalar, o, xcp[:, c, :, 0:L], conv_w[:, c, 0:1], conv_b[:, c:c + 1],
                  ALU.mult, ALU.add, after=[e])
            for k in range(1, DC):
                e = V(v.scalar_tensor_tensor, o, xcp[:, c, :, k:k + L], conv_w[:, c, k:k + 1], o,
                      ALU.mult, ALU.add, after=[e])
            yield SILU
            done["xs", c] = A(xs[:, c], xs[:, c], ACT.Silu, after=[e])
            s = yield from m_ring.take()
            t = PE(s.ap, w_in[:, (2 + c) * P:(3 + c) * P], xnT[:], True, True, after=s.before, signal=True)
            done["zs", c] = A(zs[:, c], s.ap, ACT.Silu, after=[t])
            s.free = [done["zs", c]]
            yield

        def x_proj():
            marks = []
            for c in range(CH):
                marks.append((yield from until(("xs", c))))
            s = yield from m_ring.take()
            for c in range(CH):
                t = PE(s.ap[0:DR], w_dtr[:, c], xs[:, c], c == 0, c == 1, after=marks + s.before, signal=c == 1)
            s.free = [A(dtr, s.ap[0:DR], ACT.Copy, after=[t])]
            done["dtr"] = s.free[0]
            s = yield from m_ring.take()
            for c in range(CH):
                t = PE(s.ap[0:96], w_bc3[:, c], xs[:, c], c == 0, c == 1, after=s.before, signal=c == 1)
            e0 = A(bch, s.ap[0:96], ACT.Copy, after=[t])
            e = V(v.tensor_tensor, bcr, s.ap[0:96], bch, ALU.subtract, after=[e0])
            s.free = [e]
            e1 = V(v.tensor_copy, bcm, bcr, after=[e])
            e = V(v.tensor_tensor, bcr, bcr, bcm, ALU.subtract, after=[e1])
            V(v.tensor_copy, bch[32:64], bcm[32:64], after=[e1])
            done["split"] = V(v.tensor_copy, bch[64:96], bcr[64:96], after=[e])
            yield

        def dt_proj(c):
            ready = yield from until("dtr")
            s = yield from m_ring.take()
            t = PE(s.ap, w_dt[:, c * P:(c + 1) * P], dtr, True, True, after=[ready] + s.before, signal=True)
            e = V(v.tensor_scalar, dtv[:, c], s.ap, dt_b[:, c:c + 1], None, ALU.add, after=[t])
            s.free = [e]
            e = V(v.scalar_tensor_tensor, tmp[:, c], dtv[:, c], -1.0, dtv[:, c], ALU.mult, ALU.min, after=[e])
            yield LN_EXP
            e = A(tmp[:, c], tmp[:, c], ACT.Exp, after=[e])
            e = A(tmp[:, c], tmp[:, c], ACT.Ln, bias=one_b[:, 0:1], after=[e])
            done["dt", c] = V(v.scalar_tensor_tensor, dtv[:, c], dtv[:, c], 0.0, tmp[:, c], ALU.max, ALU.add, after=[e])
            done["du", c] = V(v.tensor_tensor, du[:, c], dtv[:, c], xs[:, c], ALU.mult, after=[done["dt", c], done["xs", c]])
            yield

        def spread(q, which, ring):
            split = yield from until("split")
            dst = yield from ring.take()
            for k in range(NG):
                s = yield from m_ring.take()
                n = which * NS + q * NG + k
                t = PE(s.ap, bc(sel[:, n:n + 1], [96, P]), bch, True, True, after=[split] + s.before, signal=True)
                s.free = [A(dst.ap[:, k], s.ap, ACT.Copy, after=[t] + dst.before)]
                yield
            done["bc", which, q] = (dst, s.free[0], [])

        def scan(q, c):
            dt_done = yield from until(("dt", c))
            du_done = yield from until(("du", c))
            a_s = yield from dA.take()
            for k in range(NG):
                n = q * NG + k
                e = A(a_s.ap[:, k], dtv[:, c], ACT.Exp, scale=a_neg[:, c, n:n + 1], after=[dt_done] + a_s.before)
            z = G(g.memset, a_s.ap.rearrange("p n (s l) -> p n s l", s=2)[:, :, :, 0:1], 0.0, after=[e])
            yield
            B_s, b_done, b_read = yield from until(("bc", 0, q))
            h_s = yield from hB.take()
            bx = V(v.tensor_tensor, h_s.ap, B_s.ap, bc(du[:, c:c + 1, :], [P, NG, T]), ALU.mult,
                   after=[du_done, b_done] + h_s.before)
            b_read.append(bx)
            if len(b_read) == CH:
                B_s.free = b_read
            hf = flat2(h_s.ap)
            sc = V(v.tensor_tensor_scan, hf, flat2(a_s.ap), hf, 0.0, ALU.mult, ALU.add, after=[bx, z])
            a_s.free = [sc]
            yield
            C_s, c_done, c_read = yield from until(("bc", 1, q))
            hc = V(v.tensor_tensor, h_s.ap, h_s.ap, C_s.ap, ALU.mult, after=[sc, c_done])
            c_read.append(hc)
            if len(c_read) == CH:
                C_s.free = c_read
            yield
            while q and ("y", q - 1, c) not in done:
                yield HELD
            for k in range(NG):
                n = q * NG + k
                t = PE(y_bank[c], ident[:], h_s.ap[:, k], n == 0, n == NS - 1, after=[hc], signal=k == NG - 1)
            h_s.free = [t]
            done["y", q, c] = t
            yield

        def mamba_out():
            marks = []
            for c in range(CH):
                y = yield from until(("y", NS // NG - 1, c))
                e = V(v.scalar_tensor_tensor, xs[:, c], xs[:, c], d_skip[:, c:c + 1], y_bank[c],
                      ALU.mult, ALU.add, after=[y])
                marks.append(V(v.tensor_tensor, xs[:, c], xs[:, c], zs[:, c], ALU.mult, after=[e, done["zs", c]]))
            s = yield from m_ring.take()
            for tt in range(TT):
                for c in range(CH):
                    t = PE(s.ap[:, tt * P:(tt + 1) * P], xs[:, c, tt * P:(tt + 1) * P], w_mo[:, c], c == 0, c == 1,
                           after=marks + s.before, signal=tt == TT - 1)
            e = V(v.tensor_tensor, x1[:], x[:], tiles(s.ap), ALU.add, after=[t])
            s.free = [e]
            yield
            mark = yield from until(("moe", NE))
            e = V(v.tensor_tensor, x1[:], x1[:], moe, ALU.add, after=[e, mark])
            r = yield from layernorm(x1[:], xn[:], [e])
            s = yield from m_ring.take()
            t = transpose4(s.ap, xn[:], [r] + s.before)
            s.free = [V(v.tensor_copy, xnT[:], s.ap, after=[t])]
            yield

        def router():
            ready = yield from until("xnT")
            s = yield from ye_ring.take()
            for tt in range(TT):
                t = PE(s.ap[:, tt * NE:(tt + 1) * NE], xnT[:, tt * P:(tt + 1) * P], gate[:], True, True,
                       after=[ready] + s.before, signal=tt == TT - 1)
            lgp = s.ap[:, 0:TT * NE].rearrange("p (t e) -> p t e", t=TT)
            e = V(v.tensor_reduce, r4[:, 0], lgp, AX.X, ALU.max, after=[t])
            e = V(v.tensor_tensor, lg, lgp, bc(r4[:, 0].unsqueeze(2), [P, TT, NE]), ALU.subtract, after=[e])
            s.free = [e]
            yield LN_EXP
            f = A(ex, lg, ACT.Exp, after=[e])
            e = V(v.scalar_tensor_tensor, keyt, lg, 0.0, bc(rank[:].unsqueeze(1), [P, TT, NE]), ALU.is_equal, ALU.mult, after=[e])
            e = V(v.tensor_reduce, r4[:, 1], keyt, AX.X, ALU.max, after=[e])
            e = V(v.tensor_tensor, keyt, keyt, bc(r4[:, 1].unsqueeze(2), [P, TT, NE]), ALU.is_equal, after=[e])
            e = V(v.tensor_reduce, r4[:, 2], ex, AX.X, ALU.add, after=[f])
            e = V(v.reciprocal, r4[:, 3], r4[:, 2], after=[e])
            done["me"] = V(v.tensor_tensor, me, keyt, bc(r4[:, 3].unsqueeze(2), [P, TT, NE]), ALU.mult, after=[e])
            yield
            s = yield from ye_ring.take()
            for tt in range(TT):
                t = TR(s.ap[0:NE, tt * P:(tt + 1) * P], me[:, tt], after=[done["me"]] + s.before, signal=tt == TT - 1)
            s.free = [A(meT, s.ap[0:NE], ACT.Copy, after=[t])]
            c = s.free[0]
            yield
            s = yield from ye_ring.take()
            for tt in range(TT):
                t = PE(s.ap[:, tt * P:(tt + 1) * P], meT[:, tt * P:(tt + 1) * P], b2[:], True, True,
                       after=[c] + s.before, signal=tt == TT - 1)
            s.free = [A(moe, tiles(s.ap), ACT.Copy, after=[t])]
            done["moe", 0] = s.free[0]
            yield

        def expert(x_):
            ready = yield from until("xnT")
            h_s = yield from hT.take()
            marks = []
            for j in range(FJ):
                s = yield from h_ring.take()
                t = PE(s.ap, w1[:, x_, j * P:(j + 1) * P], xnT[:], True, True, after=[ready] + s.before, signal=True)
                s.free = [A(h_s.ap[:, j], s.ap, ACT.Relu, bias=b1[:, x_, j:j + 1], after=[t] + h_s.before)]
                marks += s.free
                yield
            s = yield from ye_ring.take()
            for tt in range(TT):
                for j in range(FJ):
                    t = PE(s.ap[:, tt * P:(tt + 1) * P], h_s.ap[:, j, tt * P:(tt + 1) * P], w2[:, x_, j], j == 0,
                           j == FJ - 1, after=[marks[j]] + s.before, signal=tt == TT - 1 and j == FJ - 1)
            h_s.free = [t]
            yield
            me_done = yield from until("me")
            acc = yield from until(("moe", x_))
            p_s = yield from prod.take()
            s.free = [V(v.tensor_tensor, p_s.ap, tiles(s.ap), bc(me[:, :, x_:x_ + 1], [P, TT, DM]), ALU.mult,
                        after=[t, me_done] + p_s.before)]
            p_s.free = [G(g.tensor_tensor, moe, moe, p_s.ap, ALU.add, after=[s.free[0], acc])]
            done["moe", x_ + 1] = p_s.free[0]
            yield

        a1 = Arena()
        gqkv = a1.get(TT, 3 * DM)
        gpad = ring_of([a1.get(HB, HB * 32) for _ in range(2)])
        gqT = a1.get(HB, T)
        gkT = a1.get(HB, T)
        ss = a1.get(TT, 2 * GH)
        cl = ring_of([a1.get(HB, 512)])
        la = ring_of([a1.get(HB, 512) for _ in range(2)])
        n_c = a1.get(TT, GH)
        vt = a1.get(TT, GH, GD + 2)
        gfac = a1.get(2, TT, GH)
        go = a1.get(TT, DM)
        goT = flat2(gpad.slots[0].ap)
        ho = gpad.slots[1].ap
        xd = a1.get(TT, DM)
        hT1 = a1.get(2, L)
        qkr = a1.get(TT, 2, LH, LD)
        raw = ring_of([a1.get(2, LH, LD) for _ in range(1)])
        rb_ = ring_of([a1.get(2, LH, LD) for _ in range(1)])
        lss = a1.get(TT, 2 * LH)
        qT = a1.get(LH // 2, T)
        kT = a1.get(LH // 2, T)
        vv = a1.get(TT, LH, LD + 1)
        SH = 4
        sm = ring_of([a1.get(SH, SW) for _ in range(2)])
        mx = ring_of([a1.get(2, SH) for _ in range(2)])
        PT = ring_of([a1.get(3, P) for _ in range(2)])
        rs = ring_of([a1.get(4) for _ in range(2)])
        qf = qkr.rearrange("p t w h e -> p (t w h e)")
        oT = qf[:, 0:4 * T].rearrange("p (j t) -> p j t", j=4)
        oo = qf[:, 4 * T:8 * T].rearrange("p (t f) -> p t f", t=TT)
        hn = raw.slots[0].ap.rearrange("p w h e -> p (w h e)")[:, 0:T].rearrange("p (t d) -> p t d", t=TT)
        hid = qf[:, 0:3 * T].rearrange("p (j t) -> p j t", j=3)
        ga = ring_of([qf[:, 3 * T:4 * T], qf[:, 4 * T:5 * T]])
        s_ring = ring_of(banks[0:2])
        av_ring = ring_of([banks[2]])
        l_ring = ring_of(banks[3:6])
        o_ring = ring_of(banks[6:8])

        def geo_qkv():
            for tt in range(TT):
                s = yield from s_ring.take()
                t = PE(s.ap[:, 0:3 * DM], xnT[:, tt * P:(tt + 1) * P], w_gqkv[:], True, True, after=s.before, signal=True)
                e = V(v.tensor_tensor, gqkv[:, tt], s.ap[:, 0:3 * DM], b_gqkv[:], ALU.add, after=[t])
                s.free = [e]
                yield
            sq_ = cl.slots[0].ap.rearrange("p a b -> p (a b)")[:, 0:TT * 2 * DM]
            ssf = flat2(ss)
            e = G(g.tensor_tensor, sq_.rearrange("p (t f) -> p t f", t=TT), gqkv[:, :, 0:2 * DM], gqkv[:, :, 0:2 * DM], ALU.mult, after=[e])
            yield
            e = V(v.tensor_reduce, ssf, sq_.rearrange("p (n e) -> p n e", e=GD), AX.X, ALU.add, after=[e])
            e = V(v.tensor_scalar, ssf, ssf, 1e-24, None, ALU.max, after=[e])
            yield SQRT
            e = A(ssf, ssf, ACT.Sqrt, after=[e])
            done["norm"] = V(v.reciprocal, ssf, ssf, after=[e])
            for s in gpad.slots:
                z = G(g.memset, s.ap, 0.0)
            done["pad"] = z
            done["one"] = G(g.memset, vt[:, :, :, GD + 1:GD + 2], 1.0)
            yield

        def geo_heads(tt, w, dst):
            nrm = yield from until("norm")
            s = yield from gpad.take()
            e = V(v.tensor_tensor, s.ap.rearrange("p a (b c) -> p (a b) c", c=32)[:, :, 0:GD],
                  gqkv[:, tt, w * DM:(w + 1) * DM].rearrange("p (h e) -> p h e", e=GD),
                  bc(ss[:, tt, w * GH:(w + 1) * GH].unsqueeze(2), [P, GH, GD]), ALU.mult,
                  after=[nrm, done["pad"]] + s.before)
            b = yield from s_ring.take()
            for hb in range(HB):
                t = TR(b.ap[:, hb * P:(hb + 1) * P], s.ap[:, hb], after=[e] + b.before, signal=hb == HB - 1)
            s.free = [t]
            yield
            b.free = [A(dst[:, :, tt * P:(tt + 1) * P], b.ap.rearrange("p (a t) -> p a t", a=HB), ACT.Copy, after=[t])]
            done["heads", tt, w] = b.free[0]
            yield

        def geo_block(b, hb):
            ready = []
            for tt in (2 * b, 2 * b + 1):
                for w in range(2):
                    ready.append((yield from until(("heads", tt, w))))
            c_s = yield from cl.take()
            for hi in range(HB):
                s = yield from s_ring.take()
                for kt in range(2):
                    t = PE(s.ap[:, kt * L:(kt + 1) * L],
                           gkT[32 * hi:32 * hi + GD, hb, b * L + kt * P:b * L + (kt + 1) * P],
                           gqT[32 * hi:32 * hi + GD, hb, b * L:(b + 1) * L], True, True,
                           after=ready + s.before, signal=kt == 1)
                e = V(v.tensor_scalar, c_s.ap[:, hi], s.ap, -1.0 + 1e-7, 1.0 - 1e-7, ALU.max, ALU.min,
                      after=[t] + c_s.before)
                s.free = [e]
                yield LN_EXP if hi == HB - 1 else None
            a_s = yield from la.take()
            f = A(a_s.ap, c_s.ap, ACT.Ln, bias=one_b[:, 0:1], after=[e] + a_s.before)
            f = A(c_s.ap, c_s.ap, ACT.Ln, bias=one_b[:, 0:1], scale=-1.0, after=[f])
            u = G(g.tensor_tensor, a_s.ap, a_s.ap, c_s.ap, ALU.subtract, after=[f])
            c_s.free = [u]
            yield TANH_ATAN
            f = A(a_s.ap, a_s.ap, ACT.Tanh, scale=0.25, after=[u])
            f = A(a_s.ap, a_s.ap, ACT.Arctan, after=[f])
            yield LN_EXP
            f = A(a_s.ap, a_s.ap, ACT.Ln, bias=one_b[:, 1:2], scale=-2.0, after=[f])
            f = A(a_s.ap, a_s.ap, ACT.Exp, scale=-3.2, after=[f])
            yield
            hs = slice(hb * HB, (hb + 1) * HB)
            nd = n_c[:, 2 * b:2 * b + 2, hs]
            e = V(v.tensor_reduce, nd.rearrange("p k h -> p h k"), a_s.ap.rearrange("p h (k s) -> p h k s", k=2),
                  AX.X, ALU.add, after=[f])
            e = V(v.reciprocal, vt[:, 2 * b:2 * b + 2, hs, GD], nd, after=[e])
            for kt in range(2):
                tt = 2 * b + kt
                e2 = V(v.tensor_tensor, vt[:, tt, hs, 0:GD],
                       gqkv[:, tt, 2 * DM:3 * DM].rearrange("p (h e) -> p h e", e=GD)[:, hs],
                       bc(vt[:, tt, hs, GD:GD + 1], [P, HB, GD]), ALU.mult, after=[e])
            yield
            if hb == 0:
                done["av", b] = yield from av_ring.take()
            o_s = yield from until(("av", b))
            while hb and ("avd", b, hb - 1) not in done:
                yield HELD
            for hi in range(HB):
                h = hb * HB + hi
                for st in range(2):
                    o = o_s.ap[:, (st * GH + h) * (GD + 2):(st * GH + h + 1) * (GD + 2)]
                    for kt in range(2):
                        t = PE(o, a_s.ap[:, hi, kt * L + st * P:kt * L + (st + 1) * P], vt[:, 2 * b + kt, h],
                               kt == 0, kt == 1, after=[e2, done["one"]] + o_s.before, signal=hi == HB - 1)
            a_s.free = [t]
            done["avd", b, hb] = t
            yield

        def geo_norm(b):
            t = yield from until(("avd", b, HB - 1))
            s = done["av", b]
            r = s.ap[:, 0:2 * GH * (GD + 2)].rearrange("p (s h e) -> p s h e", s=2, e=GD + 2)
            rr, dn = gfac[:, 0, 2 * b:2 * b + 2], gfac[:, 1, 2 * b:2 * b + 2]
            e = V(v.reciprocal, rr, r[:, :, :, GD + 1], after=[t])
            e = V(v.tensor_tensor, dn, r[:, :, :, GD], rr, ALU.mult, after=[e])
            e = V(v.tensor_scalar, dn, dn, 1e-12, None, ALU.max, after=[e])
            e = V(v.reciprocal, dn, dn, after=[e])
            e = V(v.tensor_tensor, dn, dn, rr, ALU.mult, after=[e])
            for st in range(2):
                e2 = V(v.tensor_tensor, go[:, 2 * b + st].rearrange("p (h e) -> p h e", e=GD), r[:, st, :, 0:GD],
                       bc(dn[:, st].unsqueeze(2), [P, GH, GD]), ALU.mult, after=[e])
            s.free = [e2]
            done["go", b] = e2
            yield

        def geo_out():
            yield from until(("go", 0))
            e2 = yield from until(("go", 1))
            s = yield from s_ring.take()
            t = transpose4(s.ap, go, [e2] + s.before)
            c = A(goT, s.ap, ACT.Copy, after=[t])
            s.free = [c]
            yield
            s = yield from s_ring.take()
            for tt in range(TT):
                t = PE(s.ap[:, tt * P:(tt + 1) * P], goT[:, tt * P:(tt + 1) * P], w_go[:], True, True,
                       after=[c] + s.before, signal=tt == TT - 1)
            e = V(v.tensor_tensor, ho, tiles(s.ap), bc(b_go[:].unsqueeze(1), [P, TT, DM]), ALU.add, after=[t])
            s.free = [e]
            done["geo"] = G(g.tensor_tensor, ho, ho, x1[:], ALU.add, after=[e])
            yield

        hflat = flat2(hT1)

        def shifted(src, after):
            z0 = G(g.memset, hT1[64:128, :, 0:1], 0.0, after=after)
            s = yield from l_ring.take()
            t = transpose4(s.ap, src, after + s.before)
            b = s.ap.rearrange("p (s l) -> p s l", s=2)
            A(hT1[0:64], b[0:64], ACT.Copy, after=[t])
            e = A(hT1[64:128, :, 1:L], b[64:128, :, 0:L - 1], ACT.Copy, after=[z0])
            s.free = [e]
            return e

        def loc_shift(l):
            after = [] if l == 0 else [(yield from until(("xd", l)))]
            if l == 0:
                done["vone"] = G(g.memset, vv[:, :, :, LD:LD + 1], 1.0)
            done["h", l] = yield from shifted(xn[:] if l == 0 else xd, after)
            yield

        def loc_qkv(l, tt):
            h_done = yield from until(("h", l))
            lhs = hflat[:, tt * P:(tt + 1) * P]
            r_s = yield from raw.take()
            for w in range(2):
                s = yield from l_ring.take()
                t = PE(s.ap, lhs, w_lqkv[:, l, w * INNER:(w + 1) * INNER], True, True, after=[h_done] + s.before, signal=True)
                c = A(r_s.ap[:, w], s.ap.rearrange("p (h e) -> p h e", e=LD), ACT.Copy, after=[t] + r_s.before)
                s.free = [c]
            yield
            s = yield from l_ring.take()
            t = PE(s.ap, lhs, w_lqkv[:, l, 2 * INNER:3 * INNER], True, True, after=s.before, signal=True)
            s.free = [A(vv[:, tt, :, 0:LD], s.ap.rearrange("p (h e) -> p h e", e=LD), ACT.Copy, after=[t])]
            done["v", l] = s.free[0]
            b_s = yield from rb_.take()
            q, ra, rb, H2 = r_s.ap, qkr[:, tt], b_s.ap, LD // 2
            C, S = rot[:, l, 0, tt % 2], rot[:, l, 1, tt % 2]
            e1 = V(v.tensor_tensor, ra, q, bc(C.unsqueeze(2), [P, 2, LH, LD]), ALU.mult, after=[c])
            V(v.tensor_tensor, rb[:, :, :, 0:H2], q[:, :, :, H2:LD], bc(S[:, :, 0:H2].unsqueeze(2), [P, 2, LH, H2]),
              ALU.mult, after=b_s.before)
            e2 = V(v.tensor_tensor, rb[:, :, :, H2:LD], q[:, :, :, 0:H2], bc(S[:, :, H2:LD].unsqueeze(2), [P, 2, LH, H2]), ALU.mult)
            a = A(q, q, ACT.Square, after=[e2])
            p = G(g.tensor_tensor, ra, ra, rb, ALU.add, after=[e2])
            b_s.free = [p]
            yield
            e = V(v.tensor_reduce, lss[:, tt], q.rearrange("p w h e -> p (w h) e"), AX.X, ALU.add, after=[a])
            r_s.free = [e]
            done["rot", l, tt] = (e, p)
            yield

        def loc_norm(l):
            marks = []
            for tt in range(TT):
                marks += yield from until(("rot", l, tt))
            lf = flat2(lss)
            e = V(v.tensor_scalar, lf, lf, 1e-24, None, ALU.max, after=marks)
            yield SQRT
            e = A(lf, lf, ACT.Sqrt, after=[e])
            done["lnorm", l] = V(v.reciprocal, lf, lf, after=[e])
            yield

        def loc_heads(l, tt):
            nrm = yield from until(("lnorm", l))
            e = V(v.tensor_tensor, qkr[:, tt], qkr[:, tt], bc(lss[:, tt].rearrange("p (w h) -> p w h", w=2).unsqueeze(3), [P, 2, LH, LD]),
                  ALU.mult, after=[nrm])
            for w, dst in ((0, qT), (1, kT)):
                b = yield from l_ring.take()
                for hp in range(LH // 2):
                    t = TR(b.ap[:, hp * P:(hp + 1) * P], flat2(qkr[:, tt, w, 2 * hp:2 * hp + 2]),
                           after=[e] + b.before, signal=hp == 3)
                b.free = [A(dst[:, :, tt * P:(tt + 1) * P], b.ap.rearrange("p (a t) -> p a t", a=4), ACT.Copy, after=[t])]
                done["qk", l, tt, w] = b.free[0]
                yield

        def loc_attend(l, b, h4):
            ready = []
            for tt in range(TT):
                for w in range(2):
                    ready.append((yield from until(("qk", l, tt, w))))
            m_s = yield from sm.take()
            for hh in range(SH):
                h = SH * h4 + hh
                s = yield from l_ring.take()
                pr = slice(64 * (h % 2), 64 * (h % 2) + 64)
                PE(s.ap[:, 0:P], qT[pr, h // 2, b * L:b * L + P], kT[pr, h // 2, b * L:b * L + P], True, True,
                   after=ready + s.before)
                t = PE(s.ap[:, P:SW], qT[pr, h // 2, b * L + P:(b + 1) * L], kT[pr, h // 2, b * L:(b + 1) * L], True, True, signal=True)
                e = V(v.tensor_tensor, m_s.ap[:, hh], s.ap[:, 0:SW], mask[:], ALU.add, after=[t] + m_s.before)
                s.free = [e]
                yield
            x_s = yield from mx.take()
            q0, q1 = m_s.ap[:, :, 0:P], m_s.ap[:, :, P:SW]
            V(v.tensor_reduce, x_s.ap[:, 0], q0, AX.X, ALU.max, after=[e] + x_s.before)
            e = V(v.tensor_reduce, x_s.ap[:, 1], q1, AX.X, ALU.max)
            V(v.tensor_tensor, q0, q0, bc(x_s.ap[:, 0].unsqueeze(2), [P, SH, P]), ALU.subtract, after=[e])
            e = V(v.tensor_tensor, q1, q1, bc(x_s.ap[:, 1].unsqueeze(2), [P, SH, L]), ALU.subtract)
            x_s.free = [e]
            yield LN_EXP
            f = A(m_s.ap, m_s.ap, ACT.Exp, after=[e])
            yield
            ob = []
            while sum(s.free is not None for s in o_ring.slots) < 2:
                yield HELD
            for _ in range(2):
                ob.append((yield from o_ring.take()))
            E1 = LD + 1
            for hh in range(SH):
                h = SH * h4 + hh
                s = yield from l_ring.take()
                pt = yield from PT.take()
                for k in range(3):
                    t = TR(s.ap[:, k * P:(k + 1) * P], m_s.ap[:, hh, k * P:(k + 1) * P], after=[f] + s.before, signal=k == 2)
                tr_last = t
                src = s.ap[:, 0:SW].rearrange("p (k t) -> p k t", k=3)
                c = A(pt.ap, src, ACT.Copy, after=[t] + pt.before)
                s.free = [c]
                yield
                PE(ob[0].ap[:, hh * E1:(hh + 1) * E1], pt.ap[:, 0], vv[:, 2 * b, h], True, True,
                   after=[c, done["v", l], done["vone"]] + ob[0].before)
                PE(ob[1].ap[:, hh * E1:(hh + 1) * E1], pt.ap[:, 1], vv[:, 2 * b, h], True, False, after=ob[1].before)
                t = PE(ob[1].ap[:, hh * E1:(hh + 1) * E1], pt.ap[:, 2], vv[:, 2 * b + 1, h], False, True, signal=True)
                pt.free = [t]
            m_s.free = [tr_last]
            yield
            r_s = yield from rs.take()
            before = r_s.before
            for k in range(2):
                r = ob[k].ap[:, 0:4 * E1].rearrange("p (h e) -> p h e", e=E1)
                e = V(v.reciprocal, r_s.ap, r[:, :, LD], after=[t] + before)
                e = V(v.tensor_tensor, oo[:, 2 * b + k, h4 * SH * LD:(h4 + 1) * SH * LD].rearrange("p (h e) -> p h e", e=LD),
                      r[:, :, 0:LD], bc(r_s.ap.unsqueeze(2), [P, 4, LD]), ALU.mult, after=[e])
                before = [e]
                ob[k].free = [e]
            r_s.free = [e]
            done["oo", l, b, h4] = e
            yield

        def loc_oT(l, b, k):
            yield from until(("oo", l, b, 0))
            e = yield from until(("oo", l, b, 1))
            s = yield from l_ring.take()
            tt = 2 * b + k
            for j in range(4):
                t = TR(s.ap[:, j * P:(j + 1) * P], oo[:, tt, j * P:(j + 1) * P], after=[e, done["oo", l, b, 0]] + s.before, signal=j == 3)
            s.free = [A(oT[:, :, tt * P:(tt + 1) * P], s.ap.rearrange("p (a t) -> p a t", a=4), ACT.Copy, after=[t])]
            done["oT", l, tt] = s.free[0]
            yield

        def loc_ffn(l):
            marks = []
            for tt in range(TT):
                marks.append((yield from until(("oT", l, tt))))
            s = yield from l_ring.take()
            for tt in range(TT):
                for j in range(4):
                    t = PE(s.ap[:, tt * P:(tt + 1) * P], oT[:, j, tt * P:(tt + 1) * P], w_lo[:, l, j], j == 0, j == 3,
                           after=marks + s.before, signal=tt == TT - 1)
            state = xn[:] if l == 0 else xd
            e = V(v.tensor_tensor, xd, state, tiles(s.ap), ALU.add, after=[t])
            s.free = [e]
            yield
            h_done = yield from shifted(xd, [e])
            yield
            s = yield from l_ring.take()
            for tt in range(TT):
                t = TR(s.ap[:, tt * P:(tt + 1) * P], hflat[:, tt * P:(tt + 1) * P], after=[h_done] + s.before, signal=tt == TT - 1)
            nd = yield from layernorm(tiles(s.ap), hn, [t])
            s.free = [nd]
            p = G(g.tensor_tensor, xd, xd, bc(f_b2[:, l:l + 1], [P, TT, DM]), ALU.add, after=[h_done])
            yield
            s = yield from l_ring.take()
            t = transpose4(s.ap, hn, [nd] + s.before)
            h2 = V(v.tensor_scalar, hflat, s.ap, ln_g[:, l:l + 1], ln_b[:, l:l + 1], ALU.mult, ALU.add, after=[t])
            s.free = [h2]
            yield GELU
            hd = []
            for j in range(3):
                c0, mm = j * P, HC[j]
                s = yield from l_ring.take()
                t = PE(s.ap[0:mm], f_w1[:, l, HID + c0:HID + c0 + mm], hflat, True, True, after=[h2] + s.before, signal=True)
                gs = yield from ga.take()
                a = A(gs.ap[0:mm], s.ap[0:mm], ACT.Gelu, bias=f_b1[0:mm, l, 1, j:j + 1], after=[t] + gs.before)
                s.free = [a]
                s = yield from l_ring.take()
                t = PE(s.ap[0:mm], f_w1[:, l, c0:c0 + mm], hflat, True, True, after=s.before, signal=True)
                e = V(v.scalar_tensor_tensor, hid[0:mm, j], s.ap[0:mm], f_b1[0:mm, l, 0, j:j + 1], gs.ap[0:mm],
                      ALU.add, ALU.mult, after=[t, a])
                s.free = gs.free = [e]
                hd.append(e)
            yield
            s = yield from l_ring.take()
            for tt in range(TT):
                for j in range(3):
                    t = PE(s.ap[:, tt * P:(tt + 1) * P], hid[0:HC[j], j, tt * P:(tt + 1) * P], f_w2[0:HC[j], l, j], j == 0, j == 2,
                           after=[hd[j]] + s.before, signal=tt == TT - 1)
            e = V(v.tensor_tensor, xd, xd, tiles(s.ap), ALU.add, after=[t, p])
            s.free = [e]
            done["xd", l + 1] = e
            yield

        with nc.Fori(0, NPAIR) as i:
            done.clear()
            xr = m.dma("sp", "x", x[:], d["x"][bass.ds(i, 1)].rearrange("a (t p) f -> p (a t) f", p=P))
            groups = range(NS // NG)
            run(m,
                (1, [first(xr)]),
                (2, [mamba_in(0), mamba_in(1)]),
                (1, [x_proj()]),
                (2, [dt_proj(0), dt_proj(1)]),
                (1, [spread(q, 0, Bb) for q in groups]),
                (1, [spread(q, 1, Cb) for q in groups]),
                (2, [scan(q, c) for q in groups for c in range(CH)]),
                (1, [mamba_out()]),
                (1, [router()]),
                (2, [expert(k) for k in range(NE)]))
            fence()
            done.clear()
            run(m,
                (1, [loc_shift(l) for l in range(LAY)]),
                (2, [loc_qkv(l, tt) for l in range(LAY) for tt in range(TT)]),
                (1, [loc_norm(l) for l in range(LAY)]),
                (2, [loc_heads(l, tt) for l in range(LAY) for tt in range(TT)]),
                (2, [loc_attend(l, b, h4) for l in range(LAY) for b in range(2) for h4 in range(2)]),
                (2, [loc_oT(l, b, k) for l in range(LAY) for b in range(2) for k in range(2)]),
                (1, [loc_ffn(l) for l in range(LAY)]),
                (1, [geo_qkv()]),
                (2, [geo_heads(tt, w, dst) for tt in range(TT) for w, dst in ((0, gqT), (1, gkT))]),
                (2, [geo_block(b, hb) for b in range(2) for hb in range(HB)]),
                (1, [geo_norm(0), geo_norm(1)]),
                (1, [geo_out()]))
            e = V(v.tensor_tensor, ho, ho, xd, ALU.add, after=[done["geo"], done["xd", LAY]])
            o = m.dma("sp", "out", out[bass.ds(i, 1)].rearrange("a (t p) f -> p (a t) f", p=P), ho, after=[e])
            m.wait("sp", [o])
            fence()
    return nc


def host_layout(a):
    f = lambda n: np.asarray(a[n])
    rep = lambda v_: np.broadcast_to(v_, (P,) + v_.shape)
    halves = lambda v_: v_.reshape(CH, P, *v_.shape[1:]).swapaxes(0, 1)
    r = {}
    r["x"] = f("L0_attn_x").reshape(NPAIR, T, DM)
    r["in_projT"] = f("L0_attn_in_proj_w").T
    r["conv_w"] = halves(f("L0_attn_conv_w")[:, 0])
    r["conv_b"] = halves(f("L0_attn_conv_b"))
    xp = f("L0_attn_x_proj_w").T
    r["x_projT_dt"] = halves(xp[:, :DR])
    r["x_projT_bc3"] = halves(np.concatenate([xp[:, DR:]] * 3, 1))
    r["dt_projT"] = f("L0_attn_dt_proj_w").T
    r["dt_b"] = halves(f("L0_attn_dt_proj_b"))
    r["A_log"] = halves(f("L0_attn_A_log"))
    r["D"] = halves(f("L0_attn_D"))
    r["out_projT"] = halves(f("L0_attn_out_proj_w").T)
    r["gateT"] = f("L0_ffn_gate_w").T
    r["w1"] = f("L0_ffn_w1").transpose(1, 0, 2)
    r["b1"] = f("L0_ffn_b1").reshape(NE, FJ, P).transpose(2, 0, 1)
    r["w2"] = f("L0_ffn_w2").reshape(NE, FJ, P, DM).transpose(2, 0, 1, 3)
    r["b2"] = f("L0_ffn_b2")
    r["g_qkvT"] = f("L1_attn_w_qkv").T
    r["g_b_qkv"] = rep(f("L1_attn_b_qkv"))
    r["g_outT"] = f("L1_attn_w_out").T
    r["g_b_out"] = rep(f("L1_attn_b_out"))
    r["l_wqkv"] = f("L1_ffn_wqkv").transpose(1, 0, 2)
    r["l_wo"] = f("L1_ffn_wo").reshape(LAY, INNER // P, P, DM).transpose(2, 0, 1, 3)
    r["l_ln_g"] = f("L1_ffn_ln_g").T
    r["l_ln_b"] = f("L1_ffn_ln_b").T
    r["l_w1"] = f("L1_ffn_w1").transpose(1, 0, 2)
    b = np.zeros((LAY, 2, 3, P), np.float32)
    w = np.zeros((LAY, 3, P, DM), np.float32)
    for j, n in enumerate(HC):
        for k in range(2):
            b[:, k, j, :n] = f("L1_ffn_b1")[:, k * HID + j * P:k * HID + j * P + n]
        w[:, j, :n] = f("L1_ffn_w2")[:, j * P:j * P + n]
    r["l_b1"] = b.transpose(3, 0, 1, 2)
    r["l_w2"] = w.transpose(2, 0, 1, 3)
    r["l_b2"] = rep(f("L1_ffn_b2"))
    qs, ks = f("L1_ffn_q_scale"), f("L1_ffn_k_scale")
    swap = lambda s: np.concatenate([s[:, LD // 2:], s[:, :LD // 2]], 1)
    r["qk_scale"] = rep(np.stack([np.stack([qs, ks], 1), np.stack([swap(qs), swap(ks)], 1)], 1))
    r.update(constants())
    return {k: np.ascontiguousarray(v_) for k, v_ in r.items()}


def constants():
    r = {"ident": np.eye(P, dtype=np.float32)}
    r["rank"] = np.broadcast_to((NE - np.arange(NE)).astype(np.float32), (P, NE))
    r["sel"] = np.tile(np.eye(2 * NS, dtype=np.float32), (3, 1))
    idx = np.arange(0, LD, 2, dtype=np.float32)
    inv = (1.0 / np.float32(10000.0) ** (idx / np.float32(LD))).astype(np.float32)
    t = np.arange(L, dtype=np.float32)
    fr = (t[:, None] * inv[None]).astype(np.float32)
    fr = np.concatenate([fr, fr], 1)
    base = ((idx + 0.4 * LD) / (1.4 * LD)).astype(np.float32)
    sc = base[None] ** ((t - L // 2) / float(WIN // 2)).astype(np.float32)[:, None]
    sc = np.concatenate([sc, sc], 1).astype(np.float32)
    sign = np.where(np.arange(LD) < LD // 2, -1.0, 1.0)
    fr = fr.astype(np.float64)
    tabs = np.stack([8 * np.cos(fr) * sc, np.cos(fr) / sc, 8 * np.sin(fr) * sc * sign, np.sin(fr) / sc * sign])
    tabs = tabs.astype(np.float32).reshape(2, 2, 2, P, LD).transpose(3, 0, 2, 1, 4)
    r["rot"] = np.broadcast_to(tabs[:, None], (P, LAY, 2, 2, 2, LD))
    i = np.arange(P)[:, None]
    m0 = (i - np.arange(P)[None])
    m1 = (i + P - np.arange(L)[None])
    d_ = np.concatenate([m0, m1], 1)
    r["mask"] = np.where((d_ < 0) | (d_ > WIN), np.float32(NEG), np.float32(0)).astype(np.float32)
    return r


def kernel(**inputs):
    import concourse.bacc as _bacc
    from concourse.bass_utils import run_bass_kernel_spmd as _run

    nc = _bacc.Bacc("TRN2", target_bir_lowering=False, num_devices=1)
    arrays = host_layout(inputs)
    d = {k: nc.dram_tensor("in_" + k, a.shape, mybir.dt.from_np(a.dtype), kind="ExternalInput").ap() for k, a in arrays.items()}
    out = nc.dram_tensor("out", (NPAIR, T, DM), F32, kind="ExternalOutput").ap()
    build(nc, d, out)
    r = _run(nc, [{"in_" + k: a for k, a in arrays.items()}], core_ids=[0])
    return r.results[0]["out"].reshape(SEQS, L, DM)
```
